# Optimizing a Trainium2 kernel written in Bass

```python
import numpy as np
import jax
import jax.numpy as jnp

def _softmax(x, axis=-1):
    return jax.nn.softmax(x, axis=axis)

def _gelu(x):
    return jax.nn.gelu(x, approximate=True)

def _silu(x):
    return jax.nn.silu(x)

def _sigmoid(x):
    return jax.nn.sigmoid(x)

def _layernorm(x, axis=-1, eps=1e-05):
    m = jnp.mean(x, axis=axis, keepdims=True)
    v = jnp.var(x, axis=axis, keepdims=True)
    return (x - m) / jnp.sqrt(v + eps)

def _scatter_add(tgt, idx, src, axis=0):
    return tgt.at[idx].add(src)

def _segment_sum(src, seg, n):
    return jax.ops.segment_sum(src, seg, n)
kernel_name = 'mk_rec_standalone_d1_rec_r8_ce83c1'

def setup_inputs(seed: int=0):
    np.random.seed(seed)
    _w = jnp.asarray

    def _rec_inputs():
        import jax
        import jax.numpy as jnp
        _rk = jax.random.key(seed)
        r_tokens = jax.random.randint(jax.random.fold_in(_rk, 1), (512, 256), 0, 3, jnp.int32)
        r_lengths = jax.random.randint(jax.random.fold_in(_rk, 2), (512,), 15, 2044, jnp.int32)
        return (r_tokens, r_lengths)
    r_tokens, r_lengths = _rec_inputs()

    def _L0_rec_setup():
        import jax, jax.numpy as jnp
        import numpy as np
        B, S, E, H, L = (128, 256, 256, 256, 2)
        PAD_INDEX = 2
        key = jax.random.key(seed)
        ks = jax.random.split(key, 14)
        s = 1.0 / np.sqrt(H)

        def w(k, shape):
            return jax.random.uniform(k, shape, jnp.float32, -s, s)
        emb = jax.random.normal(ks[0], (3, E), jnp.float32)
        emb = emb.at[PAD_INDEX].set(0.0)
        return {'tokens': jax.random.randint(ks[1], (B, S), 0, 3), 'lengths': jax.random.randint(ks[2], (B,), 1, S + 1), 'emb': emb, 'Wih0': w(ks[3], (H, E)), 'Whh0': w(ks[4], (H, H)), 'bih0': w(ks[5], (H,)), 'bhh0': w(ks[6], (H,)), 'Wih1': w(ks[7], (H, H)), 'Whh1': w(ks[8], (H, H)), 'bih1': w(ks[9], (H,)), 'bhh1': w(ks[10], (H,)), 'Wc': w(ks[11], (1, H)), 'bc': w(ks[12], (1,))}
    _L0_rec_all = _L0_rec_setup()
    _L0_rec_in = {k: v for k, v in _L0_rec_all.items() if k in ('emb', 'Wih0', 'Whh0', 'bih0', 'bhh0', 'Wih1', 'Whh1', 'bih1', 'bhh1', 'Wc', 'bc')}
    del _L0_rec_all
    return {'r_tokens': r_tokens, 'r_lengths': r_lengths, 'L0_rec_emb': _L0_rec_in['emb'], 'L0_rec_Wih0': _L0_rec_in['Wih0'], 'L0_rec_Whh0': _L0_rec_in['Whh0'], 'L0_rec_bih0': _L0_rec_in['bih0'], 'L0_rec_bhh0': _L0_rec_in['bhh0'], 'L0_rec_Wih1': _L0_rec_in['Wih1'], 'L0_rec_Whh1': _L0_rec_in['Whh1'], 'L0_rec_bih1': _L0_rec_in['bih1'], 'L0_rec_bhh1': _L0_rec_in['bhh1'], 'L0_rec_Wc': _L0_rec_in['Wc'], 'L0_rec_bc': _L0_rec_in['bc']}

def reference(r_tokens, r_lengths, L0_rec_emb, L0_rec_Wih0, L0_rec_Whh0, L0_rec_bih0, L0_rec_bhh0, L0_rec_Wih1, L0_rec_Whh1, L0_rec_bih1, L0_rec_bhh1, L0_rec_Wc, L0_rec_bc):
    import jax
    import jax.numpy as jnp

    def _L0_rec_ref(tokens, lengths, emb, Wih0, Whh0, bih0, bhh0, Wih1, Whh1, bih1, bhh1, Wc, bc):
        import jax, jax.numpy as jnp
        import numpy as np
        B, S, E, H, L = (128, 256, 256, 256, 2)
        PAD_INDEX = 2
        b, steps = tokens.shape
        embedded = emb[tokens]
        mask = (jnp.arange(steps)[:, None] < lengths[None, :])[:, :, None]
        params = [(Wih0, Whh0, bih0, bhh0), (Wih1, Whh1, bih1, bhh1)]

        def step(states, inp):
            x_t, m_t = inp
            cur = x_t
            new_states = []
            for layer, (Wih, Whh, bih, bhh) in enumerate(params):
                h = jnp.tanh(cur @ Wih.T + bih + states[layer] @ Whh.T + bhh)
                h = jnp.where(m_t, h, states[layer])
                new_states.append(h)
                cur = h
            return (tuple(new_states), None)
        init = tuple((jnp.zeros((b, H), embedded.dtype) for _ in range(L)))
        xs = (jnp.swapaxes(embedded, 0, 1), mask)
        states, _ = jax.lax.scan(step, init, xs)
        logits = (states[-1] @ Wc.T + bc)[:, 0]
        return logits
    y = _L0_rec_ref(r_tokens, r_lengths, L0_rec_emb, L0_rec_Wih0, L0_rec_Whh0, L0_rec_bih0, L0_rec_bhh0, L0_rec_Wih1, L0_rec_Whh1, L0_rec_bih1, L0_rec_bhh1, L0_rec_Wc, L0_rec_bc)
    return y

_drawn_inputs = setup_inputs


def setup_inputs(seed=0):
    import zlib

    import numpy as np

    out = dict(_drawn_inputs(seed))
    spreads = {}
    factors = {}
    for name, (base, spread) in spreads.items():
        noise = np.random.default_rng([zlib.crc32(name.encode()), seed]).standard_normal(out[name].shape)
        drawn = base * np.exp(spread * noise) if base else spread * noise
        out[name] = jnp.asarray(drawn.astype(out[name].dtype))
    for name, factor in factors.items():
        out[name] = (out[name] * factor).astype(out[name].dtype)
    return out
```

```python
from contextlib import ExitStack

import concourse.bass as bass
from concourse import mybir

ALU = mybir.AluOpType
ACT = mybir.ActivationFunctionType
F32 = mybir.dt.float32
F32R = mybir.dt.float32r
BF16 = mybir.dt.bfloat16
I16 = mybir.dt.int16
I32 = mybir.dt.int32

P = 128
QUAD = 32
BLOCK = 8


def build_rnn(nc, tokens_t, lengths, emb_t, wih0_t, whh0_t, wih1_t, whh1_t,
              bih0, bhh0, bih1, bhh1, wc_t, bc, row_select, out):
    STEPS, BATCH = tokens_t.shape
    HID = whh0_t.shape[0]
    VOCAB = emb_t.shape[1]
    KT = HID // P
    ROWS = VOCAB * QUAD
    REPS = QUAD // BLOCK
    NBLOCKS = STEPS // BLOCK
    assert BATCH == 512 and HID == KT * P and STEPS == NBLOCKS * BLOCK and ROWS <= P and BLOCK % 2 == 0

    with ExitStack() as ctx:
        def sb(name, shape, dt):
            return ctx.enter_context(nc.sbuf_tensor(name, shape, dt))

        def sem(name):
            return ctx.enter_context(nc.semaphore(name))

        pre0 = ctx.enter_context(nc.psum_tensor("pre0", [P, 2, KT, BATCH], F32))
        pre1 = ctx.enter_context(nc.psum_tensor("pre1", [P, 2, KT, BATCH], F32))

        names = ("whh0", "wih1", "whh1")
        w_dram = dict(zip(names, (whh0_t, wih1_t, whh1_t)))
        w_raw = {n: sb(f"{n}_raw", [P, KT, HID], F32) for n in names}
        w_hi = {n: sb(f"{n}_hi", [P, KT, HID], F32R) for n in names}
        w_lo = {n: sb(f"{n}_lo", [P, KT, HID], F32R) for n in names}
        wih0_sb = sb("wih0_sb", [P, KT, HID], F32)
        emb_sb = sb("emb_sb", [P, KT, VOCAB], F32)
        emb_rows = sb("emb_rows", [P, KT, ROWS], F32)
        bih0_rows = sb("bih0_rows", [ROWS, HID], F32)
        bhh0_rows = sb("bhh0_rows", [ROWS, HID], F32)
        bias0_rows = sb("bias0_rows", [ROWS, HID], F32)
        bih1_col = sb("bih1_col", [P, KT], F32)
        bhh1_col = sb("bhh1_col", [P, KT], F32)
        bias1_col = sb("bias1_col", [P, KT], F32)
        wc_col = sb("wc_col", [P, KT], F32)
        bc_sb = sb("bc_sb", [1, 1], F32)
        select_sb = sb("select_sb", [ROWS, 2, BLOCK], F32)
        table = sb("table", [ROWS, HID], F32)
        table_hi = sb("table_hi", [ROWS, HID], F32R)
        table_lo = sb("table_lo", [ROWS, HID], F32)
        step_table_hi = sb("step_table_hi", [ROWS, BLOCK, HID], F32)
        step_table = sb("step_table", [ROWS, BLOCK, HID], F32R)

        tokens_sb = sb("tokens_sb", [ROWS, BATCH], I32)
        row_value = sb("row_value", [ROWS, 1], F32)
        onehot = sb("onehot", [ROWS, BATCH], F32R)

        lengths_sb = sb("lengths_sb", [P, BATCH], I32)
        left = sb("left", [P, BATCH], BF16)
        is_last = sb("is_last", [P, 2, BATCH], I16)

        h0_hi = sb("h0_hi", [P, 2, KT, BATCH], F32R)
        h0_lo = sb("h0_lo", [P, 2, KT, BATCH], F32R)
        h1_hi = sb("h1_hi", [P, 2, KT, BATCH], F32R)
        h1_lo = sb("h1_lo", [P, 2, KT, BATCH], F32R)
        last_h1 = sb("last_h1", [P, KT, BATCH], F32)
        logits = sb("logits", [1, BATCH], F32)

        weights_in = sem("weights_in")
        smalls_in = sem("smalls_in")
        tokens_in = sem("tokens_in")
        emb_spread = sem("emb_spread")
        table_product = sem("table_product")
        setup_step = sem("setup_step")
        setup_done = sem("setup_done")
        onehot_ready = sem("onehot_ready")
        pre0_ready = sem("pre0_ready")
        pre1_ready = sem("pre1_ready")
        tanh0_done = sem("tanh0_done")
        tanh1_done = sem("tanh1_done")
        h0_split = sem("h0_split")
        h1_split = sem("h1_split")
        mask_ready = sem("mask_ready")
        left_ready = sem("left_ready")
        picked = sem("picked")
        logits_ready = sem("logits_ready")
        out_ready = sem("out_ready")
        out_stored = sem("out_stored")

        SMALLS = 10
        ZEROED = 2
        assert ZEROED == KT
        as_f32 = lambda ap: ap.bitcast(F32)

        def tile_of(dram):
            return dram.rearrange("(c p) n -> p c n", p=P)

        def spread(dram, rows):
            return dram.rearrange("(a n) -> a n", a=1).broadcast_to([rows, dram.shape[0]])

        def block_rows(first):
            return tokens_t[bass.ds(first, BLOCK), :].rearrange("(a s) b -> a s b", a=1).broadcast_to(
                [VOCAB * REPS, BLOCK, BATCH])

        block = ctx.enter_context(nc.Block())

        @block.sync
        def _(sp):
            sp.dma_start(tokens_sb[:], tokens_t[0:1, :].broadcast_to([ROWS, BATCH])).then_inc(tokens_in, 16)
            sp.dma_start(wih0_sb[:], tile_of(wih0_t)).then_inc(smalls_in, 16)
            for n in names:
                sp.dma_start(w_raw[n][:], tile_of(w_dram[n])).then_inc(weights_in, 16)
            with sp.Fori(0, NBLOCKS - 1) as j:
                sp.wait_ge(onehot_ready, j + 1)
                sp.dma_start(tokens_sb[:], block_rows(j * BLOCK + 1)).then_inc(tokens_in, 16)
            sp.wait_ge(onehot_ready, NBLOCKS)
            sp.dma_start(tokens_sb[:], block_rows(STEPS - BLOCK)).then_inc(tokens_in, 16)
            sp.wait_ge(out_ready, 1)
            sp.dma_start(out.rearrange("(a n) -> a n", a=1), logits[:]).then_inc(out_stored, 16)
            sp.wait_ge(out_stored, 16)

        @block.tensor
        def _(pe):
            def multiply(psum, weights, m, hi, lo, first, last):
                cols = slice(m * P, (m + 1) * P)
                terms = [(w_hi[weights][:, c, cols], lo[:, c, :]) for c in range(KT)]
                terms += [(w_lo[weights][:, c, cols], hi[:, c, :]) for c in range(KT)]
                terms += [(w_hi[weights][:, c, cols], hi[:, c, :]) for c in range(KT)]
                for i, (w, h) in enumerate(terms):
                    mm = nc.tensor.matmul(psum, w, h, start=(first and i == 0),
                                          stop=(last and i == len(terms) - 1))
                return mm

            def token_term(psum, s, m, alone):
                return nc.tensor.matmul(psum, step_table[:, s, m * P:(m + 1) * P], onehot[:],
                                        start=True, stop=alone)

            pe.wait_ge(emb_spread, 1)
            pe.wait_ge(smalls_in, 16 * SMALLS)
            for c in range(KT):
                mm = nc.tensor.matmul(pre1[0:ROWS, 0, 0, 0:HID], emb_rows[:, c, :], wih0_sb[:, c, :],
                                      start=(c == 0), stop=(c == KT - 1))
            mm.then_inc(table_product, 1)

            pe.wait_ge(setup_done, 1)
            pe.wait_ge(onehot_ready, 1)
            for m in range(KT):
                token_term(pre0[:, 0, m, :], 0, m, True).then_inc(pre0_ready, 1)

            def step(j, s, with_layer0, table_step):
                t = j * BLOCK + s
                now, nxt = s % 2, (s + 1) % 2
                pe.wait_ge(h0_split, KT * t + KT)
                if with_layer0:
                    if s == 0:
                        pe.wait_ge(onehot_ready, j + 2)
                    for m in range(KT):
                        psum = pre0[:, nxt, m, :]
                        token_term(psum, table_step, m, False)
                        multiply(psum, "whh0", m, h0_hi[:, now], h0_lo[:, now],
                                 False, True).then_inc(pre0_ready, 1)
                pe.wait_ge(picked, ZEROED + t - 1)
                for m in range(KT):
                    psum = pre1[:, now, m, :]
                    multiply(psum, "wih1", m, h0_hi[:, now], h0_lo[:, now], True, False)
                    if m == 0:
                        pe.wait_ge(h1_split, ZEROED + KT * t)
                    multiply(psum, "whh1", m, h1_hi[:, nxt], h1_lo[:, nxt],
                             False, True).then_inc(pre1_ready, 1)

            with pe.Fori(0, NBLOCKS - 1) as j:
                for s in range(BLOCK):
                    step(j, s, True, s)
            for s in range(BLOCK):
                step(NBLOCKS - 1, s, s < BLOCK - 1, (s + 1) % BLOCK)

            pe.wait_ge(picked, ZEROED + STEPS)
            for c in range(KT):
                mm = nc.tensor.matmul(pre0[0:1, 0, 0, :], wc_col[:, c:c + 1], last_h1[:, c, :],
                                      start=(c == 0), stop=(c == KT - 1))
            mm.then_inc(logits_ready, 1)

        @block.scalar
        def _(act):
            act.dma_start(emb_sb[:], tile_of(emb_t)).then_inc(smalls_in, 16)
            act.dma_start(bih0_rows[:], spread(bih0, ROWS)).then_inc(smalls_in, 16)
            act.dma_start(bhh0_rows[:], spread(bhh0, ROWS)).then_inc(smalls_in, 16)
            act.dma_start(select_sb[:], row_select).then_inc(smalls_in, 16)
            act.dma_start(lengths_sb[:], spread(lengths, P)).then_inc(smalls_in, 16)
            act.dma_start(bih1_col[:], bih1).then_inc(smalls_in, 16)
            act.dma_start(bhh1_col[:], bhh1).then_inc(smalls_in, 16)
            act.dma_start(wc_col[:], wc_t).then_inc(smalls_in, 16)
            act.dma_start(bc_sb[:], bc.rearrange("(a n) -> a n", a=1)).then_inc(smalls_in, 16)
            act.wait_ge(setup_done, 1)

            def tanh_tile(psum, hi, bias, done):
                nc.scalar.activation(hi, psum, ACT.Tanh, bias=bias)
                nc.scalar.activation(psum, psum, ACT.Tanh, bias=bias).then_inc(done, 1)

            def layer0(t, parity):
                for m in range(KT):
                    act.wait_ge(pre0_ready, KT * t + m + 1)
                    tanh_tile(pre0[:, parity, m, :], h0_hi[:, parity, m, :], 0.0, tanh0_done)

            def layer1(t, parity):
                for m in range(KT):
                    act.wait_ge(pre1_ready, KT * t + m + 1)
                    tanh_tile(pre1[:, parity, m, :], h1_hi[:, parity, m, :], bias1_col[:, m:m + 1],
                              tanh1_done)

            layer0(0, 0)
            with act.Fori(0, NBLOCKS - 1) as j:
                for s in range(BLOCK):
                    layer0(j * BLOCK + s + 1, (s + 1) % 2)
                    layer1(j * BLOCK + s, s % 2)
            for s in range(BLOCK):
                t = (NBLOCKS - 1) * BLOCK + s
                if s < BLOCK - 1:
                    layer0(t + 1, (s + 1) % 2)
                layer1(t, s % 2)

            act.wait_ge(logits_ready, 1)
            nc.scalar.activation(logits[:], pre0[0:1, 0, 0, :], ACT.Identity,
                                 bias=bc_sb[:]).then_inc(out_ready, 1)

        @block.vector
        def _(dve):
            steps_done = [0]

            def setup(ins):
                steps_done[0] += 1
                ins.then_inc(setup_step, 1)
                dve.wait_ge(setup_step, steps_done[0])

            def one_hot(n):
                dve.wait_ge(tokens_in, n * 16)
                nc.vector.tensor_scalar(onehot[:], tokens_sb[:], row_value[:], None,
                                        ALU.is_equal).then_inc(onehot_ready, 1)

            for v in range(VOCAB):
                nc.vector.memset(row_value[v * QUAD:(v + 1) * QUAD, :], float(v))
            for part in (h1_hi, h1_lo):
                nc.vector.memset(as_f32(part[:, 1]), 0.0).then_inc(h1_split, 1)
            for m in range(KT):
                last = nc.vector.memset(last_h1[:, m], 0.0).then_inc(picked, 1)
            dve.wait_ge(picked, ZEROED)
            one_hot(1)

            dve.wait_ge(smalls_in, 16 * SMALLS)
            for c in range(KT):
                for v in range(VOCAB):
                    e = nc.vector.tensor_copy(emb_rows[:, c, v * QUAD:(v + 1) * QUAD],
                                              emb_sb[:, c, v:v + 1].broadcast_to([P, QUAD]))
            e.then_inc(emb_spread, 1)

            nc.vector.tensor_tensor(bias1_col[:], bih1_col[:], bhh1_col[:], ALU.add)
            nc.vector.tensor_scalar(left[:], lengths_sb[:], float(STEPS), 0.0, ALU.min,
                                    ALU.max).then_inc(left_ready, 1)
            setup(nc.vector.tensor_tensor(bias0_rows[:], bih0_rows[:], bhh0_rows[:], ALU.add))

            dve.wait_ge(table_product, 1)
            setup(nc.vector.tensor_tensor(table[:], pre1[0:ROWS, 0, 0, 0:HID], bias0_rows[:], ALU.add))
            setup(nc.vector.tensor_copy(table_hi[:], table[:]))
            setup(nc.vector.tensor_tensor(table_lo[:], table[:], as_f32(table_hi[:]), ALU.subtract))
            for s in range(BLOCK):
                last = nc.vector.tensor_scalar(step_table_hi[:, s, :], as_f32(table_hi[:]),
                                               select_sb[:, 0, s:s + 1], None, ALU.mult)
            setup(last)
            for s in range(BLOCK):
                nc.vector.scalar_tensor_tensor(
                    out=step_table[:, s, :], in0=table_lo[:], scalar=select_sb[:, 1, s:s + 1],
                    in1=step_table_hi[:, s, :], op0=ALU.mult, op1=ALU.add)

            dve.wait_ge(weights_in, 16 * len(names))
            for n in names:
                last = nc.vector.tensor_copy(w_hi[n][:], w_raw[n][:])
            setup(last)
            for n in names:
                last = nc.vector.tensor_tensor(w_lo[n][:], w_raw[n][:], as_f32(w_hi[n][:]), ALU.subtract)
            last.then_inc(setup_done, 1)

            def split_tile(psum, hi, lo, done):
                nc.vector.tensor_tensor(lo, psum, as_f32(hi), ALU.subtract).then_inc(done, 1)

            def layer0(t, parity):
                for m in range(KT):
                    dve.wait_ge(tanh0_done, KT * t + m + 1)
                    split_tile(pre0[:, parity, m, :], h0_hi[:, parity, m, :], h0_lo[:, parity, m, :],
                               h0_split)

            def layer1(j, s):
                t, parity = j * BLOCK + s, s % 2
                if s == 0:
                    dve.wait_ge(left_ready, j + 1)
                nc.vector.tensor_scalar(is_last[:, parity, :], left[:], float(s + 1), None,
                                        ALU.is_equal).then_inc(mask_ready, 1)
                if s == BLOCK - 1:
                    nc.vector.tensor_scalar(left[:], left[:], float(BLOCK), None,
                                            ALU.subtract).then_inc(left_ready, 1)
                for m in range(KT):
                    if m == KT - 1:
                        dve.wait_ge(mask_ready, t + 1)
                        dve.wait_ge(picked, ZEROED + t)
                    dve.wait_ge(tanh1_done, KT * t + m + 1)
                    split_tile(pre1[:, parity, m, :], h1_hi[:, parity, m, :], h1_lo[:, parity, m, :],
                               h1_split)
                mask = is_last[:, parity:parity + 1, :].broadcast_to([P, KT, BATCH])
                nc.vector.copy_predicated(last_h1[:], mask, pre1[:, parity]).then_inc(picked, 1)

            layer0(0, 0)
            one_hot(2)
            with dve.Fori(0, NBLOCKS - 1) as j:
                for s in range(BLOCK):
                    layer0(j * BLOCK + s + 1, (s + 1) % 2)
                    if s == BLOCK - 1:
                        one_hot(j + 3)
                    layer1(j, s)
            for s in range(BLOCK):
                j = NBLOCKS - 1
                if s < BLOCK - 1:
                    layer0(j * BLOCK + s + 1, (s + 1) % 2)
                layer1(j, s)


def kernel(r_tokens, r_lengths, L0_rec_emb, L0_rec_Wih0, L0_rec_Whh0, L0_rec_bih0, L0_rec_bhh0,
           L0_rec_Wih1, L0_rec_Whh1, L0_rec_bih1, L0_rec_bhh1, L0_rec_Wc, L0_rec_bc):
    import numpy as np
    import concourse.bacc as bacc
    from concourse.bass_utils import run_bass_kernel_spmd

    vocab, hid = L0_rec_emb.shape

    def columns(v):
        return np.ascontiguousarray(np.asarray(v).reshape(hid // P, P).T)

    row_select = np.zeros((vocab * QUAD, 2, BLOCK), np.float32)
    for row in range(vocab * QUAD):
        repeat, s = row % QUAD // BLOCK, row % BLOCK
        if repeat < 2:
            row_select[row, repeat, s] = 1.0

    arrays = {
        "tokens_t": np.ascontiguousarray(np.asarray(r_tokens).T),
        "lengths": np.asarray(r_lengths),
        "emb_t": np.ascontiguousarray(np.asarray(L0_rec_emb).T),
        "wih0_t": np.ascontiguousarray(np.asarray(L0_rec_Wih0).T),
        "whh0_t": np.ascontiguousarray(np.asarray(L0_rec_Whh0).T),
        "wih1_t": np.ascontiguousarray(np.asarray(L0_rec_Wih1).T),
        "whh1_t": np.ascontiguousarray(np.asarray(L0_rec_Whh1).T),
        "bih0": np.asarray(L0_rec_bih0),
        "bhh0": np.asarray(L0_rec_bhh0),
        "bih1": columns(L0_rec_bih1),
        "bhh1": columns(L0_rec_bhh1),
        "wc_t": columns(L0_rec_Wc),
        "bc": np.asarray(L0_rec_bc),
        "row_select": row_select,
    }
    nc = bacc.Bacc("TRN2", target_bir_lowering=False, num_devices=1)
    args = [nc.dram_tensor(name, a.shape, mybir.dt.from_np(a.dtype), kind="ExternalInput").ap()
            for name, a in arrays.items()]
    out = nc.dram_tensor("logits_out", (arrays["lengths"].shape[0],), F32, kind="ExternalOutput").ap()
    build_rnn(nc, *args, out)
    result = run_bass_kernel_spmd(nc, [arrays], core_ids=[0])
    return result.results[0]["logits_out"]
```

```python
from contextlib import ExitStack

import concourse.bass as bass
from concourse import mybir

ALU = mybir.AluOpType
ACT = mybir.ActivationFunctionType
F32 = mybir.dt.float32
F32R = mybir.dt.float32r
BF16 = mybir.dt.bfloat16
I16 = mybir.dt.int16
I32 = mybir.dt.int32

P = 128
BLOCK = 8
SLOTS = 4
BIG = 2.0 ** 30


def build_rnn(nc, tokens_t, lengths, emb_t, wih0_t, whh0_t, wih1_t, whh1_t,
              bih0, bhh0, bih1, bhh1, wc_t, bc, codes_dram, out):
    STEPS, BATCH = tokens_t.shape
    HID = whh0_t.shape[0]
    VOCAB = emb_t.shape[1]
    KT = HID // P
    NBLOCKS = STEPS // BLOCK
    TT = STEPS // P
    assert BATCH == 512 and HID == KT * P and VOCAB == 3
    assert STEPS == NBLOCKS * BLOCK == TT * P and BLOCK % SLOTS == 0 and SLOTS == 4

    with ExitStack() as ctx:
        def sb(name, shape, dt):
            return ctx.enter_context(nc.sbuf_tensor(name, shape, dt))

        def sem(name):
            return ctx.enter_context(nc.semaphore(name))

        pre0 = ctx.enter_context(nc.psum_tensor("pre0", [P, 2, KT, BATCH], F32))
        pre1 = ctx.enter_context(nc.psum_tensor("pre1", [P, 2, KT, BATCH], F32))

        names = ("whh0", "wih1", "whh1")
        w_dram = dict(zip(names, (whh0_t, wih1_t, whh1_t)))
        w_raw = {n: sb(f"{n}_raw", [P, KT, HID], F32) for n in names}
        w_hi = {n: sb(f"{n}_hi", [P, KT, HID], F32R) for n in names}
        w_lo = {n: sb(f"{n}_lo", [P, KT, HID], F32R) for n in names}
        wih0_sb = sb("wih0_sb", [P, KT, HID], F32)
        emb_sb = sb("emb_sb", [P, KT, VOCAB], F32)
        bih0_col = sb("bih0_col", [P, KT], F32)
        bhh0_col = sb("bhh0_col", [P, KT], F32)
        bias0_col = sb("bias0_col", [P, KT], F32)
        bih1_col = sb("bih1_col", [P, KT], F32)
        bhh1_col = sb("bhh1_col", [P, KT], F32)
        bias1_col = sb("bias1_col", [P, KT], F32)
        wc_col = sb("wc_col", [P, KT], F32)
        bc_sb = sb("bc_sb", [1, 1], F32)
        y = sb("y", [P, VOCAB, KT], F32)
        q_col = sb("q_col", [P, KT], F32)
        d2_col = sb("d2_col", [P, KT], F32)
        p_col = sb("p_col", [P, KT], F32)

        tokens_sb = sb("tokens_sb", [P, TT, BATCH], I32)
        is_one = sb("is_one", [P, TT, BATCH], F32)
        codes_sb = sb("codes_sb", [P, TT, 2, BATCH], BF16)
        codes = sb("codes", [P, SLOTS, 2, BATCH], BF16)
        factor = sb("factor", [P, 2, KT, BATCH], F32)
        x_term = sb("x_term", [P, 2, KT, BATCH], F32)

        lengths_sb = sb("lengths_sb", [P, BATCH], I32)
        left = sb("left", [P, BATCH], BF16)
        is_last = sb("is_last", [P, 2, BATCH], I16)

        h0_hi = sb("h0_hi", [P, 2, KT, BATCH], F32R)
        h0_lo = sb("h0_lo", [P, 2, KT, BATCH], F32R)
        h1_hi = sb("h1_hi", [P, 2, KT, BATCH], F32R)
        h1_lo = sb("h1_lo", [P, 2, KT, BATCH], F32R)
        last_h1 = sb("last_h1", [P, KT, BATCH], F32)
        logits = sb("logits", [1, BATCH], F32)

        weights_in = {n: sem(f"{n}_in") for n in names}
        inputs_in = sem("inputs_in")
        smalls_in = sem("smalls_in")
        tokens_in = sem("tokens_in")
        codes_made = sem("codes_made")
        codes_stored = sem("codes_stored")
        codes_in = [sem(f"codes_in{k}") for k in range(SLOTS)]
        y_product = sem("y_product")
        setup_step = sem("setup_step")
        x_scalars = sem("x_scalars")
        weights_split = sem("weights_split")
        bias1_ready = sem("bias1_ready")
        factor_ready = sem("factor_ready")
        x_ready = sem("x_ready")
        product0 = sem("product0")
        pre0_ready = sem("pre0_ready")
        pre1_ready = sem("pre1_ready")
        tanh0_done = sem("tanh0_done")
        tanh1_done = sem("tanh1_done")
        h0_split = sem("h0_split")
        h1_split = sem("h1_split")
        mask_ready = sem("mask_ready")
        left_ready = sem("left_ready")
        picked = sem("picked")
        logits_ready = sem("logits_ready")
        out_ready = sem("out_ready")
        out_stored = sem("out_stored")

        INPUTS, SMALLS = 4, 5
        ZEROED = 2
        assert ZEROED == KT
        as_f32 = lambda ap: ap.bitcast(F32)

        def tile_of(dram):
            return dram.rearrange("(c p) n -> p c n", p=P)

        block = ctx.enter_context(nc.Block())

        @block.sync
        def _(sp):
            sp.dma_start(tokens_sb[:], tile_of(tokens_t)).then_inc(tokens_in, 16)
            for n in names:
                sp.dma_start(w_raw[n][:], tile_of(w_dram[n])).then_inc(weights_in[n], 16)
            sp.wait_ge(codes_made, 1)
            sp.dma_start(codes_dram.rearrange("(c p) k b -> p c k b", p=P), codes_sb[:]).then_inc(codes_stored, 16)
            sp.wait_ge(codes_stored, 16)

            def load_codes(n, slot):
                sp.dma_start(codes[:, slot], codes_dram[bass.ds(n, 1)].broadcast_to([P, 2, BATCH])
                             ).then_inc(codes_in[slot], 16)

            for n in range(SLOTS):
                load_codes(n, n)
            with sp.Fori(0, STEPS // SLOTS - 1) as i:
                for k in range(SLOTS):
                    sp.wait_ge(x_ready, KT * (i * SLOTS + k + 1))
                    load_codes(i * SLOTS + (SLOTS + k), k)
            sp.wait_ge(out_ready, 1)
            sp.dma_start(out.rearrange("(a n) -> a n", a=1), logits[:]).then_inc(out_stored, 16)
            sp.wait_ge(out_stored, 16)

        @block.gpsimd
        def _(pool):
            def input_term(n, s, codes_round, first=False, last=False):
                parity, slot, next_slot = s % 2, s % SLOTS, (s + 1) % SLOTS
                for m in range(KT):
                    nc.gpsimd.tensor_scalar(factor[:, parity, m], codes[:, slot, 0], p_col[:, m:m + 1],
                                            q_col[:, m:m + 1], ALU.mult, ALU.add).then_inc(factor_ready, 1)
                if not first:
                    pool.wait_ge(tanh0_done, KT * (n - 1))
                for m in range(KT):
                    if m == KT - 1 and not last:
                        pool.wait_ge(codes_in[next_slot], 16 * codes_round)
                        if not first:
                            pool.wait_ge(x_ready, KT * n)
                    pool.wait_ge(factor_ready, KT * n + m + 1)
                    nc.gpsimd.tensor_tensor(x_term[:, parity, m], factor[:, parity, m], codes[:, slot, 1],
                                            ALU.mult).then_inc(x_ready, 1)

            pool.wait_ge(codes_in[0], 16)
            pool.wait_ge(x_scalars, 1)
            for n in range(2):
                input_term(n, n, 1, first=True)
            with pool.Fori(0, (STEPS - 2) // BLOCK) as j:
                for s in range(2, BLOCK + 2):
                    input_term(j * BLOCK + s, s, j * (BLOCK // SLOTS) + ((s + 1) // SLOTS + 1))
            for n in range(STEPS - (STEPS - 2) % BLOCK, STEPS):
                input_term(n, n, (n + 1) // SLOTS + 1, last=(n == STEPS - 1))

        @block.tensor
        def _(pe):
            def multiply(psum, weights, m, hi, lo, first, last):
                cols = slice(m * P, (m + 1) * P)
                terms = [(w_hi[weights][:, c, cols], lo[:, c, :]) for c in range(KT)]
                terms += [(w_lo[weights][:, c, cols], hi[:, c, :]) for c in range(KT)]
                terms += [(w_hi[weights][:, c, cols], hi[:, c, :]) for c in range(KT)]
                for i, (w, h) in enumerate(terms):
                    mm = nc.tensor.matmul(psum, w, h, start=(first and i == 0),
                                          stop=(last and i == len(terms) - 1))
                return mm

            pe.wait_ge(inputs_in, 16 * INPUTS)
            for m in range(KT):
                for c in range(KT):
                    mm = nc.tensor.matmul(pre1[:, 0, m, 0:VOCAB], wih0_sb[:, c, m * P:(m + 1) * P],
                                          emb_sb[:, c, :], start=(c == 0), stop=(c == KT - 1))
            mm.then_inc(y_product, 1)

            def step(j, s, with_layer0):
                t = j * BLOCK + s
                now, nxt = s % 2, (s + 1) % 2
                pe.wait_ge(h0_split, KT * t + KT)
                if with_layer0:
                    for m in range(KT):
                        multiply(pre0[:, nxt, m, :], "whh0", m, h0_hi[:, now], h0_lo[:, now],
                                 True, True).then_inc(product0, 1)
                pe.wait_ge(picked, ZEROED + t - 1)
                for m in range(KT):
                    psum = pre1[:, now, m, :]
                    multiply(psum, "wih1", m, h0_hi[:, now], h0_lo[:, now], True, False)
                    if m == 0:
                        pe.wait_ge(h1_split, ZEROED + KT * t)
                    multiply(psum, "whh1", m, h1_hi[:, nxt], h1_lo[:, nxt],
                             False, True).then_inc(pre1_ready, 1)

            pe.wait_ge(weights_split, len(names))
            with pe.Fori(0, NBLOCKS - 1) as j:
                for s in range(BLOCK):
                    step(j, s, True)
            for s in range(BLOCK):
                step(NBLOCKS - 1, s, s < BLOCK - 1)

            pe.wait_ge(picked, ZEROED + STEPS)
            for c in range(KT):
                mm = nc.tensor.matmul(pre0[0:1, 0, 0, :], wc_col[:, c:c + 1], last_h1[:, c, :],
                                      start=(c == 0), stop=(c == KT - 1))
            mm.then_inc(logits_ready, 1)

        @block.scalar
        def _(act):
            act.dma_start(wih0_sb[:], tile_of(wih0_t)).then_inc(inputs_in, 16)
            act.dma_start(emb_sb[:], tile_of(emb_t)).then_inc(inputs_in, 16)
            act.dma_start(bih0_col[:], bih0).then_inc(inputs_in, 16)
            act.dma_start(bhh0_col[:], bhh0).then_inc(inputs_in, 16)
            act.dma_start(lengths_sb[:], lengths.rearrange("(a n) -> a n", a=1).broadcast_to([P, BATCH])
                          ).then_inc(smalls_in, 16)
            act.dma_start(bih1_col[:], bih1).then_inc(smalls_in, 16)
            act.dma_start(bhh1_col[:], bhh1).then_inc(smalls_in, 16)
            act.dma_start(wc_col[:], wc_t).then_inc(smalls_in, 16)
            act.dma_start(bc_sb[:], bc.rearrange("(a n) -> a n", a=1)).then_inc(smalls_in, 16)

            def tanh_tile(source, psum, hi, bias, done):
                nc.scalar.activation(hi, source, ACT.Tanh, bias=bias)
                nc.scalar.activation(psum, source, ACT.Tanh, bias=bias).then_inc(done, 1)

            def layer0(t, parity):
                for m in range(KT):
                    act.wait_ge(pre0_ready, KT * (t - 1) + m + 1)
                    psum = pre0[:, parity, m, :]
                    tanh_tile(psum, psum, h0_hi[:, parity, m, :], bias0_col[:, m:m + 1], tanh0_done)

            def layer1(t, parity):
                for m in range(KT):
                    act.wait_ge(pre1_ready, KT * t + m + 1)
                    psum = pre1[:, parity, m, :]
                    tanh_tile(psum, psum, h1_hi[:, parity, m, :], bias1_col[:, m:m + 1], tanh1_done)

            for m in range(KT):
                act.wait_ge(x_ready, m + 1)
                tanh_tile(x_term[:, 0, m, :], pre0[:, 0, m, :], h0_hi[:, 0, m, :],
                          bias0_col[:, m:m + 1], tanh0_done)
            act.wait_ge(bias1_ready, 1)
            with act.Fori(0, NBLOCKS - 1) as j:
                for s in range(BLOCK):
                    layer0(j * BLOCK + s + 1, (s + 1) % 2)
                    layer1(j * BLOCK + s, s % 2)
            for s in range(BLOCK):
                t = (NBLOCKS - 1) * BLOCK + s
                if s < BLOCK - 1:
                    layer0(t + 1, (s + 1) % 2)
                layer1(t, s % 2)

            act.wait_ge(logits_ready, 1)
            nc.scalar.activation(logits[:], pre0[0:1, 0, 0, :], ACT.Identity,
                                 bias=bc_sb[:]).then_inc(out_ready, 1)

        @block.vector
        def _(dve):
            steps_done = [0]

            def setup(ins):
                steps_done[0] += 1
                ins.then_inc(setup_step, 1)
                dve.wait_ge(setup_step, steps_done[0])

            dve.wait_ge(tokens_in, 16)
            nc.vector.tensor_scalar(is_one[:], tokens_sb[:], 1.0, None, ALU.is_equal)
            setup(nc.vector.tensor_scalar(codes_sb[:, :, 0], tokens_sb[:], 2.0, BIG, ALU.is_equal, ALU.mult))
            nc.vector.scalar_tensor_tensor(
                out=codes_sb[:, :, 1], in0=codes_sb[:, :, 0], scalar=BIG ** -2, in1=is_one[:],
                op0=ALU.mult, op1=ALU.add).then_inc(codes_made, 1)

            dve.wait_ge(y_product, 1)
            setup(nc.vector.tensor_copy(y[:], pre1[:, 0, :, 0:VOCAB].rearrange("p m v -> p v m")))
            nc.vector.tensor_tensor(bias0_col[:], bih0_col[:], bhh0_col[:], ALU.add)
            nc.vector.tensor_tensor(d2_col[:], y[:, 2], y[:, 0], ALU.subtract)
            setup(nc.vector.tensor_tensor(q_col[:], y[:, 1], y[:, 0], ALU.subtract))
            nc.vector.tensor_tensor(bias0_col[:], bias0_col[:], y[:, 0], ALU.add)
            nc.vector.scalar_tensor_tensor(out=p_col[:], in0=q_col[:], scalar=-1.0 / BIG, in1=d2_col[:],
                                           op0=ALU.mult, op1=ALU.add).then_inc(x_scalars, 1)

            for n in names:
                dve.wait_ge(weights_in[n], 16)
                setup(nc.vector.tensor_copy(w_hi[n][:], w_raw[n][:]))
                nc.vector.tensor_tensor(w_lo[n][:], w_raw[n][:], as_f32(w_hi[n][:]),
                                        ALU.subtract).then_inc(weights_split, 1)

            for part in (h1_hi, h1_lo):
                nc.vector.memset(as_f32(part[:, 1]), 0.0).then_inc(h1_split, 1)
            for m in range(KT):
                nc.vector.memset(last_h1[:, m], 0.0).then_inc(picked, 1)
            dve.wait_ge(smalls_in, 16 * SMALLS)
            nc.vector.tensor_tensor(bias1_col[:], bih1_col[:], bhh1_col[:], ALU.add).then_inc(bias1_ready, 1)
            nc.vector.tensor_scalar(left[:], lengths_sb[:], float(STEPS), 0.0, ALU.min,
                                    ALU.max).then_inc(left_ready, 1)

            def split_state(psum, hi, lo, done):
                nc.vector.tensor_tensor(lo, psum, as_f32(hi), ALU.subtract).then_inc(done, 1)

            def add_input(t, parity, m):
                dve.wait_ge(product0, KT * (t - 1) + m + 1)
                dve.wait_ge(x_ready, KT * t + m + 1)
                psum = pre0[:, parity, m, :]
                nc.vector.tensor_tensor(psum, psum, x_term[:, parity, m, :], ALU.add).then_inc(pre0_ready, 1)

            def split0(t, parity):
                for m in range(KT):
                    dve.wait_ge(tanh0_done, KT * t + m + 1)
                    split_state(pre0[:, parity, m, :], h0_hi[:, parity, m, :], h0_lo[:, parity, m, :],
                                h0_split)

            def split1(t, parity):
                for m in range(KT):
                    dve.wait_ge(tanh1_done, KT * t + m + 1)
                    split_state(pre1[:, parity, m, :], h1_hi[:, parity, m, :], h1_lo[:, parity, m, :],
                                h1_split)

            def mask(j, s):
                if s == 0:
                    dve.wait_ge(left_ready, j + 1)
                nc.vector.tensor_scalar(is_last[:, s % 2, :], left[:], float(s + 1), None,
                                        ALU.is_equal).then_inc(mask_ready, 1)
                if s == BLOCK - 1:
                    nc.vector.tensor_scalar(left[:], left[:], float(BLOCK), None,
                                            ALU.subtract).then_inc(left_ready, 1)

            def step(j, s, more):
                t, parity = j * BLOCK + s, s % 2
                if more >= 1:
                    split0(t + 1, 1 - parity)
                mask(j, s)
                split1(t, parity)
                if more >= 2:
                    add_input(t + 2, parity, 0)
                dve.wait_ge(mask_ready, t + 1)
                dve.wait_ge(picked, ZEROED + t)
                if more >= 2:
                    for m in range(1, KT):
                        add_input(t + 2, parity, m)
                is_last_tiles = is_last[:, parity:parity + 1, :].broadcast_to([P, KT, BATCH])
                nc.vector.copy_predicated(last_h1[:], is_last_tiles, pre1[:, parity]).then_inc(picked, 1)

            split0(0, 0)
            for m in range(KT):
                add_input(1, 1, m)
            with dve.Fori(0, NBLOCKS - 1) as j:
                for s in range(BLOCK):
                    step(j, s, BLOCK)
            for s in range(BLOCK):
                step(NBLOCKS - 1, s, BLOCK - 1 - s)


def kernel(r_tokens, r_lengths, L0_rec_emb, L0_rec_Wih0, L0_rec_Whh0, L0_rec_bih0, L0_rec_bhh0,
           L0_rec_Wih1, L0_rec_Whh1, L0_rec_bih1, L0_rec_bhh1, L0_rec_Wc, L0_rec_bc):
    import numpy as np
    import concourse.bacc as bacc
    from concourse.bass_utils import run_bass_kernel_spmd

    hid = L0_rec_emb.shape[1]

    def columns(v):
        return np.ascontiguousarray(np.asarray(v).reshape(hid // P, P).T)

    arrays = {
        "tokens_t": np.ascontiguousarray(np.asarray(r_tokens).T),
        "lengths": np.asarray(r_lengths),
        "emb_t": np.ascontiguousarray(np.asarray(L0_rec_emb).T),
        "wih0_t": np.ascontiguousarray(np.asarray(L0_rec_Wih0).T),
        "whh0_t": np.ascontiguousarray(np.asarray(L0_rec_Whh0).T),
        "wih1_t": np.ascontiguousarray(np.asarray(L0_rec_Wih1).T),
        "whh1_t": np.ascontiguousarray(np.asarray(L0_rec_Whh1).T),
        "bih0": columns(L0_rec_bih0),
        "bhh0": columns(L0_rec_bhh0),
        "bih1": columns(L0_rec_bih1),
        "bhh1": columns(L0_rec_bhh1),
        "wc_t": columns(L0_rec_Wc),
        "bc": np.asarray(L0_rec_bc),
    }
    nc = bacc.Bacc("TRN2", target_bir_lowering=False, num_devices=1)
    args = [nc.dram_tensor(name, a.shape, mybir.dt.from_np(a.dtype), kind="ExternalInput").ap()
            for name, a in arrays.items()]
    out = nc.dram_tensor("logits_out", (arrays["lengths"].shape[0],), F32, kind="ExternalOutput").ap()
    steps, batch = arrays["tokens_t"].shape
    codes_dram = nc.dram_tensor("token_codes", (steps, 2, batch), BF16).ap()
    build_rnn(nc, *args, codes_dram, out)
    result = run_bass_kernel_spmd(nc, [arrays], core_ids=[0])
    return result.results[0]["logits_out"]
```
